# Optimizing a Trainium2 kernel written in Bass

```python
import numpy as np
import jax
import jax.numpy as jnp

def _softmax(x, axis=-1):
    return jax.nn.softmax(x, axis=axis)

def _gelu(x):
    return jax.nn.gelu(x, approximate=True)

def _silu(x):
    return jax.nn.silu(x)

def _sigmoid(x):
    return jax.nn.sigmoid(x)

def _layernorm(x, axis=-1, eps=1e-05):
    m = jnp.mean(x, axis=axis, keepdims=True)
    v = jnp.var(x, axis=axis, keepdims=True)
    return (x - m) / jnp.sqrt(v + eps)

def _scatter_add(tgt, idx, src, axis=0):
    return tgt.at[idx].add(src)

def _segment_sum(src, seg, n):
    return jax.ops.segment_sum(src, seg, n)
kernel_name = 'mk_dlrm_tower_d1_rec_r8_74e773'

def setup_inputs(seed: int=0):
    np.random.seed(seed)
    _w = jnp.asarray

    def _rec_inputs():
        import jax
        import jax.numpy as jnp
        _tk = jax.random.key(seed)
        dense_ctx = jax.random.normal(jax.random.fold_in(_tk, 190), (2048, 16), jnp.float32)
        ids = jnp.stack([jax.random.randint(jax.random.fold_in(_tk, 200 + f), (2048,), 0, v, jnp.int32) for f, v in enumerate([125000, 1000, 1250, 1000, 12500, 12500, 12500, 125000, 12500, 12500, 12500, 1000, 1250, 1250, 12500, 1250, 1250, 1000, 1250, 1000, 1250, 1000, 1000, 12500, 1000, 12500, 1250, 1000, 1000, 1250, 1250, 1000])], axis=1)
        tbl_0 = 0.05 * jax.random.normal(jax.random.fold_in(_tk, 500 + 0), (125000, 64), jnp.float32)
        tbl_1 = 0.05 * jax.random.normal(jax.random.fold_in(_tk, 500 + 1), (1000, 64), jnp.float32)
        tbl_2 = 0.05 * jax.random.normal(jax.random.fold_in(_tk, 500 + 2), (1250, 64), jnp.float32)
        tbl_3 = 0.05 * jax.random.normal(jax.random.fold_in(_tk, 500 + 3), (1000, 64), jnp.float32)
        tbl_4 = 0.05 * jax.random.normal(jax.random.fold_in(_tk, 500 + 4), (12500, 64), jnp.float32)
        tbl_5 = 0.05 * jax.random.normal(jax.random.fold_in(_tk, 500 + 5), (12500, 64), jnp.float32)
        tbl_6 = 0.05 * jax.random.normal(jax.random.fold_in(_tk, 500 + 6), (12500, 64), jnp.float32)
        tbl_7 = 0.05 * jax.random.normal(jax.random.fold_in(_tk, 500 + 7), (125000, 64), jnp.float32)
        tbl_8 = 0.05 * jax.random.normal(jax.random.fold_in(_tk, 500 + 8), (12500, 64), jnp.float32)
        tbl_9 = 0.05 * jax.random.normal(jax.random.fold_in(_tk, 500 + 9), (12500, 64), jnp.float32)
        tbl_10 = 0.05 * jax.random.normal(jax.random.fold_in(_tk, 500 + 10), (12500, 64), jnp.float32)
        tbl_11 = 0.05 * jax.random.normal(jax.random.fold_in(_tk, 500 + 11), (1000, 64), jnp.float32)
        tbl_12 = 0.05 * jax.random.normal(jax.random.fold_in(_tk, 500 + 12), (1250, 64), jnp.float32)
        tbl_13 = 0.05 * jax.random.normal(jax.random.fold_in(_tk, 500 + 13), (1250, 64), jnp.float32)
        tbl_14 = 0.05 * jax.random.normal(jax.random.fold_in(_tk, 500 + 14), (12500, 64), jnp.float32)
        tbl_15 = 0.05 * jax.random.normal(jax.random.fold_in(_tk, 500 + 15), (1250, 64), jnp.float32)
        tbl_16 = 0.05 * jax.random.normal(jax.random.fold_in(_tk, 500 + 16), (1250, 64), jnp.float32)
        tbl_17 = 0.05 * jax.random.normal(jax.random.fold_in(_tk, 500 + 17), (1000, 64), jnp.float32)
        tbl_18 = 0.05 * jax.random.normal(jax.random.fold_in(_tk, 500 + 18), (1250, 64), jnp.float32)
        tbl_19 = 0.05 * jax.random.normal(jax.random.fold_in(_tk, 500 + 19), (1000, 64), jnp.float32)
        tbl_20 = 0.05 * jax.random.normal(jax.random.fold_in(_tk, 500 + 20), (1250, 64), jnp.float32)
        tbl_21 = 0.05 * jax.random.normal(jax.random.fold_in(_tk, 500 + 21), (1000, 64), jnp.float32)
        tbl_22 = 0.05 * jax.random.normal(jax.random.fold_in(_tk, 500 + 22), (1000, 64), jnp.float32)
        tbl_23 = 0.05 * jax.random.normal(jax.random.fold_in(_tk, 500 + 23), (12500, 64), jnp.float32)
        tbl_24 = 0.05 * jax.random.normal(jax.random.fold_in(_tk, 500 + 24), (1000, 64), jnp.float32)
        tbl_25 = 0.05 * jax.random.normal(jax.random.fold_in(_tk, 500 + 25), (12500, 64), jnp.float32)
        tbl_26 = 0.05 * jax.random.normal(jax.random.fold_in(_tk, 500 + 26), (1250, 64), jnp.float32)
        tbl_27 = 0.05 * jax.random.normal(jax.random.fold_in(_tk, 500 + 27), (1000, 64), jnp.float32)
        tbl_28 = 0.05 * jax.random.normal(jax.random.fold_in(_tk, 500 + 28), (1000, 64), jnp.float32)
        tbl_29 = 0.05 * jax.random.normal(jax.random.fold_in(_tk, 500 + 29), (1250, 64), jnp.float32)
        tbl_30 = 0.05 * jax.random.normal(jax.random.fold_in(_tk, 500 + 30), (1250, 64), jnp.float32)
        tbl_31 = 0.05 * jax.random.normal(jax.random.fold_in(_tk, 500 + 31), (1000, 64), jnp.float32)
        _rk = jax.random.fold_in(_tk, 7)
        W_top1 = 0.0441942 * jax.random.normal(jax.random.fold_in(_tk, 801), (512, 512), jnp.float32)
        W_top2 = 0.0441942 * jax.random.normal(jax.random.fold_in(_tk, 802), (512, 256), jnp.float32)
        W_top3 = 0.0625 * jax.random.normal(jax.random.fold_in(_tk, 803), (256, 1), jnp.float32)
        b_top1 = jnp.zeros((512,), jnp.float32)
        b_top2 = jnp.zeros((256,), jnp.float32)
        return (dense_ctx, ids, tbl_0, tbl_1, tbl_2, tbl_3, tbl_4, tbl_5, tbl_6, tbl_7, tbl_8, tbl_9, tbl_10, tbl_11, tbl_12, tbl_13, tbl_14, tbl_15, tbl_16, tbl_17, tbl_18, tbl_19, tbl_20, tbl_21, tbl_22, tbl_23, tbl_24, tbl_25, tbl_26, tbl_27, tbl_28, tbl_29, tbl_30, tbl_31, W_top1, b_top1, W_top2, b_top2, W_top3)
    dense_ctx, ids, tbl_0, tbl_1, tbl_2, tbl_3, tbl_4, tbl_5, tbl_6, tbl_7, tbl_8, tbl_9, tbl_10, tbl_11, tbl_12, tbl_13, tbl_14, tbl_15, tbl_16, tbl_17, tbl_18, tbl_19, tbl_20, tbl_21, tbl_22, tbl_23, tbl_24, tbl_25, tbl_26, tbl_27, tbl_28, tbl_29, tbl_30, tbl_31, W_top1, b_top1, W_top2, b_top2, W_top3 = _rec_inputs()

    def _L0_rec_setup():
        import jax, jax.numpy as jnp
        import numpy as np
        B = 256
        NUM_FIELDS = 32
        EMBED = 64
        P = NUM_FIELDS * (NUM_FIELDS - 1) // 2
        _ROW, _COL = np.triu_indices(NUM_FIELDS, k=1)
        ROW_IDX = jnp.asarray(_ROW, dtype=jnp.int32)
        COL_IDX = jnp.asarray(_COL, dtype=jnp.int32)
        key = jax.random.key(seed)
        k1, k2 = jax.random.split(key)
        emb_inputs = jax.random.normal(k1, (B, NUM_FIELDS, EMBED), dtype=jnp.float32)
        fan_in = P * EMBED
        fan_out = EMBED
        std = float(np.sqrt(2.0 / (fan_in + fan_out)))
        kernel = jax.random.normal(k2, (EMBED, P, EMBED), dtype=jnp.float32) * std
        return {'emb_inputs': emb_inputs, 'kernel': kernel}
    _L0_rec_all = _L0_rec_setup()
    _L0_rec_in = {k: v for k, v in _L0_rec_all.items() if k in ('kernel',)}
    del _L0_rec_all
    return {'dense_ctx': dense_ctx, 'ids': ids, 'tbl_0': tbl_0, 'tbl_1': tbl_1, 'tbl_2': tbl_2, 'tbl_3': tbl_3, 'tbl_4': tbl_4, 'tbl_5': tbl_5, 'tbl_6': tbl_6, 'tbl_7': tbl_7, 'tbl_8': tbl_8, 'tbl_9': tbl_9, 'tbl_10': tbl_10, 'tbl_11': tbl_11, 'tbl_12': tbl_12, 'tbl_13': tbl_13, 'tbl_14': tbl_14, 'tbl_15': tbl_15, 'tbl_16': tbl_16, 'tbl_17': tbl_17, 'tbl_18': tbl_18, 'tbl_19': tbl_19, 'tbl_20': tbl_20, 'tbl_21': tbl_21, 'tbl_22': tbl_22, 'tbl_23': tbl_23, 'tbl_24': tbl_24, 'tbl_25': tbl_25, 'tbl_26': tbl_26, 'tbl_27': tbl_27, 'tbl_28': tbl_28, 'tbl_29': tbl_29, 'tbl_30': tbl_30, 'tbl_31': tbl_31, 'W_top1': W_top1, 'b_top1': b_top1, 'W_top2': W_top2, 'b_top2': b_top2, 'W_top3': W_top3, 'L0_rec_kernel': _L0_rec_in['kernel']}

def reference(dense_ctx, ids, tbl_0, tbl_1, tbl_2, tbl_3, tbl_4, tbl_5, tbl_6, tbl_7, tbl_8, tbl_9, tbl_10, tbl_11, tbl_12, tbl_13, tbl_14, tbl_15, tbl_16, tbl_17, tbl_18, tbl_19, tbl_20, tbl_21, tbl_22, tbl_23, tbl_24, tbl_25, tbl_26, tbl_27, tbl_28, tbl_29, tbl_30, tbl_31, W_top1, b_top1, W_top2, b_top2, W_top3, L0_rec_kernel):
    import jax
    import jax.numpy as jnp

    def _L0_rec_ref(emb_inputs, kernel):
        import jax, jax.numpy as jnp
        import numpy as np
        B = 256
        NUM_FIELDS = 32
        EMBED = 64
        P = NUM_FIELDS * (NUM_FIELDS - 1) // 2
        _ROW, _COL = np.triu_indices(NUM_FIELDS, k=1)
        ROW_IDX = jnp.asarray(_ROW, dtype=jnp.int32)
        COL_IDX = jnp.asarray(_COL, dtype=jnp.int32)
        p = emb_inputs[:, ROW_IDX]
        q = emb_inputs[:, COL_IDX]
        return jnp.einsum('bne,hne,bnh->bn', p, kernel, q)
    e = jnp.stack([tbl_0[ids[:, 0]], tbl_1[ids[:, 1]], tbl_2[ids[:, 2]], tbl_3[ids[:, 3]], tbl_4[ids[:, 4]], tbl_5[ids[:, 5]], tbl_6[ids[:, 6]], tbl_7[ids[:, 7]], tbl_8[ids[:, 8]], tbl_9[ids[:, 9]], tbl_10[ids[:, 10]], tbl_11[ids[:, 11]], tbl_12[ids[:, 12]], tbl_13[ids[:, 13]], tbl_14[ids[:, 14]], tbl_15[ids[:, 15]], tbl_16[ids[:, 16]], tbl_17[ids[:, 17]], tbl_18[ids[:, 18]], tbl_19[ids[:, 19]], tbl_20[ids[:, 20]], tbl_21[ids[:, 21]], tbl_22[ids[:, 22]], tbl_23[ids[:, 23]], tbl_24[ids[:, 24]], tbl_25[ids[:, 25]], tbl_26[ids[:, 26]], tbl_27[ids[:, 27]], tbl_28[ids[:, 28]], tbl_29[ids[:, 29]], tbl_30[ids[:, 30]], tbl_31[ids[:, 31]]], axis=1)
    z = _L0_rec_ref(e, L0_rec_kernel)
    z = z.reshape(z.shape[0], -1)
    h = jnp.concatenate([z, dense_ctx], axis=1)
    h = jnp.maximum(h @ W_top1 + b_top1, 0.0)
    h = jnp.maximum(h @ W_top2 + b_top2, 0.0)
    y = h @ W_top3
    return y

_drawn_inputs = setup_inputs


def setup_inputs(seed=0):
    import zlib

    import numpy as np

    out = dict(_drawn_inputs(seed))
    spreads = {'b_top1': (0.0, 0.1), 'b_top2': (0.0, 0.1)}
    factors = {'tbl_0': 8.0,
     'tbl_1': 8.0,
     'tbl_2': 8.0,
     'tbl_3': 8.0,
     'tbl_4': 8.0,
     'tbl_5': 8.0,
     'tbl_6': 8.0,
     'tbl_7': 8.0,
     'tbl_8': 8.0,
     'tbl_9': 8.0,
     'tbl_10': 8.0,
     'tbl_11': 8.0,
     'tbl_12': 8.0,
     'tbl_13': 8.0,
     'tbl_14': 8.0,
     'tbl_15': 8.0,
     'tbl_16': 8.0,
     'tbl_17': 8.0,
     'tbl_18': 8.0,
     'tbl_19': 8.0,
     'tbl_20': 8.0,
     'tbl_21': 8.0,
     'tbl_22': 8.0,
     'tbl_23': 8.0,
     'tbl_24': 8.0,
     'tbl_25': 8.0,
     'tbl_26': 8.0,
     'tbl_27': 8.0,
     'tbl_28': 8.0,
     'tbl_29': 8.0,
     'tbl_30': 8.0,
     'tbl_31': 8.0,
     'L0_rec_kernel': 8.0}
    for name, (base, spread) in spreads.items():
        noise = np.random.default_rng([zlib.crc32(name.encode()), seed]).standard_normal(out[name].shape)
        drawn = base * np.exp(spread * noise) if base else spread * noise
        out[name] = jnp.asarray(drawn.astype(out[name].dtype))
    for name, factor in factors.items():
        out[name] = (out[name] * factor).astype(out[name].dtype)
    return out
```

```python
from contextlib import ExitStack

import numpy as np

import concourse.bass as bass
from concourse import mybir

BATCH = 2048
FIELDS = 32
EMBED = 64
DENSE = 16
HID1 = 512
HID2 = 256

P = 128
HALVES = 2
BH = BATCH // HALVES
BT = BH // P
BANK = 512
CHUNKS = BH // BANK
STEPS = FIELDS - 1
STAGES = 8
PAIRS_COLS = FIELDS * EMBED
PRODUCTS = 8
GROUP = 4
TRANSPOSE_LEAD = 4

F32 = mybir.dt.float32
F32R = mybir.dt.float32r
I32 = mybir.dt.int32
ALU = mybir.AluOpType
ACTF = mybir.ActivationFunctionType


def tiles_of(j):
    return (j + 1) // 2


def tiles_until(j):
    return sum(tiles_of(s) for s in range(1, j + 1))


TILES = tiles_until(STEPS)
SUM_ROWS = TILES * 2
KTILES = SUM_ROWS // P
TILES_PER_KTILE = TILES // KTILES
SUMS = TILES // GROUP * CHUNKS
assert SUM_ROWS == HID1 and SUM_ROWS % P == 0


def pair_index(i, j):
    return i * (FIELDS - 1) - i * (i - 1) // 2 + (j - i - 1)


def tile_slot(t):
    return t // TILES_PER_KTILE, t % GROUP, 2 * (t % TILES_PER_KTILE // GROUP)


def rows_of_top1():
    rows, spare = np.zeros(SUM_ROWS, np.int64), []
    t = 0
    for j in range(1, FIELDS):
        for p in range(tiles_of(j)):
            q, c, r = tile_slot(t)
            at = P * q + 32 * c + r
            for s in range(2):
                if 2 * p + s < j:
                    rows[at + s] = pair_index(2 * p + s, j)
                else:
                    rows[at + s] = FIELDS * (FIELDS - 1) // 2 + len(spare)
                    spare.append(at + s)
            t += 1
    assert len(spare) == DENSE
    return rows, spare


def transpose_after(j):
    return max(0, tiles_of(j) - TRANSPOSE_LEAD)


def sum_turns_after(t):
    if t == TILES - 1:
        first = (t - 5) // 2
        return [(u // CHUNKS, u % CHUNKS) for u in range(first, SUMS)]
    if t % 2 == 1 and t >= 5:
        u = (t - 5) // 2
        return [(u // CHUNKS, u % CHUNKS)]
    return []


def field_after_ktile(q):
    last = TILES_PER_KTILE * (q + 1) + 3
    j = 1
    while tiles_until(j) <= last:
        j += 1
    inside = last - tiles_until(j - 1)
    return j + 1 if inside <= transpose_after(j) else j + 2


def tower_kernel(nc, dense_ctx, ids, tables, k_rec, w1, b1, w2, b2, w3, out):
    _, spare_rows = rows_of_top1()
    ctx = ExitStack()
    with ctx:
        def sb(name, shape, dt=F32):
            return ctx.enter_context(nc.sbuf_tensor(name, shape, dt))

        def pb(name, shape):
            return ctx.enter_context(nc.psum_tensor(name, shape, F32))

        def sem(name):
            return ctx.enter_context(nc.semaphore(name))

        pair_emb = sb("pair_emb", [P, FIELDS // 2, BH])
        emb_hi = sb("emb_hi", [P, 2, BH], F32R)
        emb_lo = sb("emb_lo", [P, 2, BH], F32R)
        k_raw = sb("k_raw", [P, 2, PAIRS_COLS])
        k_split = sb("k_split", [P, 2, PAIRS_COLS], F32R)
        zeros = sb("zeros", [P, EMBED])
        product = sb("product", [P, PRODUCTS, BH])
        stage = sb("stage", [P, STAGES, BT, EMBED])
        twice = sb("twice", [P, 2, BT, 2, EMBED])
        zt = sb("zt", [P, KTILES, BH])
        w1_sb = sb("w1_sb", [P, KTILES, HID1])
        w2_sb = sb("w2_sb", [P, HID1 // P, HID2])
        w3_sb = sb("w3_sb", [P, HID2 // P])
        b1_sb = sb("b1_sb", [P, HID1 // P])
        b2_sb = sb("b2_sb", [P, HID2 // P])
        ids_sb = sb("ids_sb", [P, BT, FIELDS], I32)
        dense_sb = sb("dense_sb", [P, BT, DENSE])
        ident = sb("ident", [P, P])
        ones_sel = sb("ones_sel", [P, 62])
        edge = sb("edge", [64, BATCH])
        dense_t = edge[0:DENSE, 0:BH]
        y_sb = edge[32:33, :]
        h1 = product[:, 0:4, :].rearrange("p (m x) b -> p m (x b)", m=HID1 // P)
        h2 = product[:, 4:6, :].rearrange("p (m x) b -> p m (x b)", m=HID2 // P)

        bilinear = [pb(f"bilinear{n}", [P, BH]) for n in range(2)]
        turned = pb("turned", [P, BH])
        sums = pb("sums", [P, BH])

        weights_in = sem("weights_in")
        ids_in = sem("ids_in")
        dense_in = sem("dense_in")
        gathered = [sem(f"gathered{s}") for s in range(STAGES)]
        k_in = [sem(f"k_in{s}") for s in range(2)]
        consts = sem("consts")
        ident_cleared = sem("ident_cleared")
        sel_cleared = sem("sel_cleared")
        dense_turned = sem("dense_turned")
        dense_copied = sem("dense_copied")
        dense_placed = sem("dense_placed")
        half_begun = sem("half_begun")
        stage_claimed = sem("stage_claimed")
        field_doubled = sem("field_doubled")
        field_turned = sem("field_turned")
        pair_ready = sem("pair_ready")
        hi_ready = sem("hi_ready")
        lo_ready = sem("lo_ready")
        k_hi_ready = sem("k_hi_ready")
        k_zeroed = sem("k_zeroed")
        k_lo_ready = sem("k_lo_ready")
        bilinear_ready = sem("bilinear_ready")
        multiplied = sem("multiplied")
        summed = sem("summed")
        z_copied = sem("z_copied")
        h1_made = sem("h1_made")
        h1_kept = sem("h1_kept")
        h2_made = sem("h2_made")
        h2_kept = sem("h2_kept")
        y_made = sem("y_made")
        y_kept = sem("y_kept")
        y_out = sem("y_out")

        ids_v = ids.rearrange("(h t p) f -> h p t f", h=HALVES, p=P)
        dense_v = dense_ctx.rearrange("(h t p) d -> h p t d", h=HALVES, p=P)

        def k_loads(j):
            return [(i, min(2, j - i)) for i in range(0, j, 2)]

        def k_loads_until(j):
            return sum(2 * len(k_loads(s)) for s in range(1, j + 1) if s % 2 == j % 2)

        K_LOADS = [k_loads_until(STEPS - 1), k_loads_until(STEPS)]
        FIELDS_PER_STAGE = FIELDS // STAGES

        block = ctx.enter_context(nc.Block())

        @block.sync
        def _(sp):
            sp.dma_start(w1_sb[:, :, :], w1.rearrange("(q p) n -> p q n", p=P)).then_inc(weights_in, 16)
            sp.dma_start(w2_sb[:, :, :], w2.rearrange("(q p) n -> p q n", p=P)).then_inc(weights_in, 16)
            with nc.allow_non_contiguous_dma(reason="a few hundred values"):
                sp.dma_start(w3_sb[:, :], w3.rearrange("(q p) o -> p (q o)", p=P)).then_inc(weights_in, 16)
                sp.dma_start(b1_sb[:, :], b1.rearrange("(q p) -> p q", p=P)).then_inc(weights_in, 16)
                sp.dma_start(b2_sb[:, :], b2.rearrange("(q p) -> p q", p=P)).then_inc(weights_in, 16)
            with sp.Fori(0, HALVES) as half:
                sp.dma_start(dense_sb[:, :, :], dense_v[half]).then_inc(dense_in, 16)
                for j in range(1, FIELDS):
                    if j >= 3:
                        sp.wait_ge(k_hi_ready, half * STEPS + j - 2)
                        sp.wait_ge(k_lo_ready, half * STEPS + j - 2)
                    for i, n in k_loads(j):
                        at = pair_index(i, j)
                        src = k_rec[:, at:at + 1, :] if n == 1 else k_rec[:, at:pair_index(i + 1, j) + 1:FIELDS - 2 - i, :]
                        if n == 2 and FIELDS - 2 - i == 0:
                            src = k_rec[:, at:at + 2, :]
                        for rows in range(2):
                            sp.dma_start(
                                k_raw[EMBED * rows:EMBED * (rows + 1), j % 2, i * EMBED:(i + n) * EMBED]
                                .rearrange("p (n e) -> p n e", e=EMBED), src).then_inc(k_in[j % 2], 16)
                sp.wait_ge(dense_copied, half + 1)
                sp.wait_ge(z_copied, half * KTILES + KTILES)
                for d, row in enumerate(spare_rows):
                    sp.dma_start(zt[row % P:row % P + 1, row // P, :],
                                 dense_t[d:d + 1, :]).then_inc(dense_placed, 16)
            sp.wait_ge(y_kept, HALVES * CHUNKS)
            sp.dma_start(out.rearrange("b o -> o b"), y_sb).then_inc(y_out, 16)
            sp.wait_ge(y_out, 16)

        @block.gpsimd
        def _(pool):
            nc.gpsimd.memset(ident[:, :], 0.0).then_inc(ident_cleared, 1)
            pool.wait_ge(ident_cleared, 1)
            nc.gpsimd.affine_select(out=ident[:, :], in_=ident[:, :], compare_op=ALU.not_equal, fill=1.0,
                                    base=0, pattern=[[-1, P]], channel_multiplier=1).then_inc(consts, 1)
            with pool.Fori(0, HALVES) as half:
                pool.dma_start(ids_sb[:, :, :], ids_v[half]).then_inc(ids_in, 16)
                pool.wait_ge(ids_in, half * 16 + 16)
                pool.sem_inc(half_begun, 1)
                for f in range(FIELDS):
                    if f >= STAGES:
                        pool.wait_ge(field_doubled, half * FIELDS + f - STAGES + 1)
                        pool.sem_inc(stage_claimed, 1)
                    for t in range(BT):
                        nc.gpsimd.indirect_dma_start(
                            stage[:, f % STAGES, t, :], None, tables[f],
                            bass.IndirectOffsetOnAxis(ap=ids_sb[:, t, f:f + 1], axis=0),
                        ).then_inc(gathered[f % STAGES], 16)
                for s in range(STAGES):
                    pool.wait_ge(gathered[s], (half + 1) * (FIELDS_PER_STAGE * BT * 16))
                pool.wait_ge(field_doubled, half * FIELDS + FIELDS)

        @block.scalar
        def _(act):
            act.wait_ge(consts, 4)
            with act.Fori(0, HALVES) as half:
                def double_field(f):
                    act.wait_ge(gathered[f % STAGES],
                                half * (FIELDS_PER_STAGE * BT * 16) + (f // STAGES + 1) * BT * 16)
                    if f >= 2:
                        act.wait_ge(field_turned, half * FIELDS + f - 1)
                    rows = stage[:, f % STAGES, :, :].rearrange("p t (a e) -> p t a e", a=1)
                    nc.scalar.activation(twice[:, f % 2, :, :, :], rows.broadcast_to([P, BT, 2, EMBED]),
                                         ACTF.Copy).then_inc(field_doubled, 1)

                def copy_k_hi(j):
                    act.wait_ge(k_in[j % 2], half * (16 * K_LOADS[j % 2]) + 16 * k_loads_until(j))
                    if j >= 3:
                        act.wait_ge(bilinear_ready, half * TILES + tiles_until(j - 2))
                    if j % 2 == 1:
                        nc.scalar.activation(k_split[:, 1, j * EMBED:(j + 1) * EMBED], zeros[:, :],
                                             ACTF.Copy).then_inc(k_zeroed, 1)
                    nc.scalar.activation(k_split[:, j % 2, 0:j * EMBED], k_raw[:, j % 2, 0:j * EMBED],
                                         ACTF.Copy).then_inc(k_hi_ready, 1)

                def copy_field(f):
                    act.wait_ge(field_turned, half * FIELDS + f + 1)
                    rows = slice(EMBED * (f % 2), EMBED * (f % 2) + EMBED)
                    nc.scalar.activation(pair_emb[rows, f // 2, :], turned[rows, :],
                                         ACTF.Copy).then_inc(pair_ready, 1)
                    if f >= 1:
                        nc.scalar.activation(emb_hi[:, f % 2, :], turned[:, :], ACTF.Copy).then_inc(hi_ready, 1)

                def copy_z(q):
                    act.wait_ge(summed, half * SUMS + SUMS // KTILES * (q + 1))
                    nc.scalar.activation(zt[:, q, :], sums[:, :], ACTF.Copy).then_inc(z_copied, 1)

                act.wait_ge(dense_turned, half + 1)
                nc.scalar.activation(dense_t, turned[0:DENSE, :], ACTF.Copy).then_inc(dense_copied, 1)
                double_field(0)
                copy_field(0)
                for f in range(1, FIELDS):
                    double_field(f)
                    copy_k_hi(f)
                    for q in range(KTILES - 1):
                        if f == field_after_ktile(q):
                            copy_z(q)
                    copy_field(f)
                copy_z(KTILES - 1)

                act.wait_ge(weights_in, 16 * 5)
                for c in range(CHUNKS):
                    for m in range(HID1 // P):
                        if m % 2 == 0:
                            act.wait_ge(h1_made, half * (CHUNKS * 4) + c * 4 + m + 1)
                            nc.scalar.activation(h1[:, m, c * BANK:(c + 1) * BANK],
                                                 bilinear[m // 2][:, (m % 2) * BANK:(m % 2 + 1) * BANK],
                                                 ACTF.Relu, bias=b1_sb[:, m:m + 1]).then_inc(h1_kept, 1)
                for c in range(CHUNKS):
                    act.wait_ge(h2_made, half * (CHUNKS * 2) + c * 2 + 1)
                    nc.scalar.activation(h2[:, 0, c * BANK:(c + 1) * BANK], turned[:, 0:BANK],
                                         ACTF.Relu, bias=b2_sb[:, 0:1]).then_inc(h2_kept, 1)

        @block.vector
        def _(dve):
            nc.vector.memset(ones_sel[:, :], 0.0).then_inc(sel_cleared, 1)
            nc.vector.memset(zeros[:, :], 0.0).then_inc(consts, 1)
            dve.wait_ge(sel_cleared, 1)
            nc.vector.memset(ones_sel[0:EMBED, 30:31], 1.0).then_inc(consts, 1)
            nc.vector.memset(ones_sel[EMBED:P, 31:32], 1.0).then_inc(consts, 1)
            with dve.Fori(0, HALVES) as half:
                def split_k_lo(j):
                    dve.wait_ge(k_hi_ready, half * STEPS + j)
                    nc.vector.tensor_tensor(
                        k_split[EMBED:P, j % 2, 0:j * EMBED], k_raw[EMBED:P, j % 2, 0:j * EMBED],
                        k_split[EMBED:P, j % 2, 0:j * EMBED].bitcast(F32), ALU.subtract).then_inc(k_lo_ready, 1)

                def split_lo(f):
                    dve.wait_ge(hi_ready, half * STEPS + f)
                    nc.vector.tensor_tensor(emb_lo[:, f % 2, :], turned[:, :], emb_hi[:, f % 2, :].bitcast(F32),
                                            ALU.subtract).then_inc(lo_ready, 1)

                split_k_lo(1)
                split_lo(1)
                t = 0
                for j in range(1, FIELDS):
                    last = tiles_of(j) - 1
                    for p in range(tiles_of(j)):
                        if p == 0:
                            dve.wait_ge(pair_ready, half * FIELDS + j + 1)
                        dve.wait_ge(bilinear_ready, half * TILES + t + 1)
                        if t >= PRODUCTS and t % GROUP == 0:
                            dve.wait_ge(summed, half * SUMS + CHUNKS * ((t - PRODUCTS) // GROUP + 1))
                        nc.vector.tensor_tensor(product[:, t % PRODUCTS, :], bilinear[t % 2][:, :],
                                                pair_emb[:, p, :], ALU.mult).then_inc(multiplied, 1)
                        if j < STEPS and p == min(3, transpose_after(j)):
                            split_k_lo(j + 1)
                        if j < STEPS and p == min(transpose_after(j) + 1, last):
                            split_lo(j + 1)
                        t += 1

                dve.wait_ge(weights_in, 16 * 5)
                for c in range(CHUNKS):
                    for m in range(HID1 // P):
                        if m % 2 == 1:
                            dve.wait_ge(h1_made, half * (CHUNKS * 4) + c * 4 + m + 1)
                            nc.vector.tensor_scalar(h1[:, m, c * BANK:(c + 1) * BANK],
                                                    bilinear[m // 2][:, (m % 2) * BANK:(m % 2 + 1) * BANK],
                                                    b1_sb[:, m:m + 1], 0.0, ALU.add, ALU.max).then_inc(h1_kept, 1)
                for c in range(CHUNKS):
                    dve.wait_ge(h2_made, half * (CHUNKS * 2) + c * 2 + 2)
                    nc.vector.tensor_scalar(h2[:, 1, c * BANK:(c + 1) * BANK], turned[:, BANK:2 * BANK],
                                            b2_sb[:, 1:2], 0.0, ALU.add, ALU.max).then_inc(h2_kept, 1)
                for c in range(CHUNKS):
                    dve.wait_ge(y_made, half * CHUNKS + c + 1)
                    nc.vector.tensor_copy(y_sb[:, bass.ds(half * BH + c * BANK, BANK)],
                                          sums[32:33, c * BANK:(c + 1) * BANK]).then_inc(y_kept, 1)

        @block.tensor
        def _(pe):
            pe.wait_ge(consts, 4)
            with pe.Fori(0, HALVES) as half:
                def transpose_field(f):
                    pe.wait_ge(field_doubled, half * FIELDS + f + 1)
                    if f == 0:
                        pe.wait_ge(dense_copied, half + 1)
                    else:
                        pe.wait_ge(pair_ready, half * FIELDS + f)
                    if f >= 2:
                        pe.wait_ge(lo_ready, half * STEPS + f - 1)
                    for t in range(BT):
                        rows = twice[:, f % 2, t, :, :].rearrange("p a e -> p (a e)")
                        last = nc.tensor.transpose(turned[:, t * P:(t + 1) * P], rows, ident[:, :])
                    last.then_inc(field_turned, 1)

                def bilinear_tile(j, p, t):
                    if p == 0:
                        pe.wait_ge(lo_ready, half * STEPS + j)
                        pe.wait_ge(k_lo_ready, half * STEPS + j)
                    if t >= 2:
                        pe.wait_ge(multiplied, half * TILES + t - 1)
                    if 2 * p + 1 == j:
                        pe.wait_ge(k_zeroed, half * (FIELDS // 2) + (j + 1) // 2)
                    weights = k_split[:, j % 2, 2 * p * EMBED:(2 * p + 2) * EMBED]
                    for c in range(CHUNKS):
                        for part, emb in enumerate((emb_lo, emb_hi)):
                            last = nc.tensor.matmul(bilinear[t % 2][:, c * BANK:(c + 1) * BANK], weights,
                                                    emb[:, j % 2, c * BANK:(c + 1) * BANK],
                                                    start=(part == 0), stop=(part == 1))
                    last.then_inc(bilinear_ready, 1)

                def sum_rows(g, c):
                    pe.wait_ge(multiplied, half * TILES + GROUP * (g + 1))
                    q, _, r = tile_slot(GROUP * g)
                    if q >= 1 and r == 0:
                        pe.wait_ge(z_copied, half * KTILES + q)
                    for n in range(GROUP):
                        last = nc.tensor.matmul(sums[32 * n:32 * n + 32, c * BANK:(c + 1) * BANK],
                                                ones_sel[:, 30 - r:62 - r],
                                                product[:, (GROUP * g + n) % PRODUCTS, c * BANK:(c + 1) * BANK],
                                                start=(r == 0), stop=(r == 30))
                    last.then_inc(summed, 1)

                pe.wait_ge(dense_in, half * 16 + 16)
                for t in range(BT):
                    last = nc.tensor.transpose(turned[0:DENSE, t * P:(t + 1) * P], dense_sb[:, t, :], ident[:, :])
                last.then_inc(dense_turned, 1)
                transpose_field(0)
                transpose_field(1)
                t = 0
                for j in range(1, FIELDS):
                    for p in range(tiles_of(j)):
                        bilinear_tile(j, p, t)
                        for g, c in sum_turns_after(t):
                            sum_rows(g, c)
                        if j < STEPS and p == transpose_after(j):
                            transpose_field(j + 1)
                        t += 1

                pe.wait_ge(weights_in, 16 * 5)
                pe.wait_ge(z_copied, half * KTILES + KTILES)
                pe.wait_ge(dense_placed, half * (16 * DENSE) + 16 * DENSE)
                for c in range(CHUNKS):
                    for m in range(HID1 // P):
                        if c >= 1:
                            pe.wait_ge(h1_kept, half * (CHUNKS * 4) + 4 * c)
                        for q in range(KTILES):
                            last = nc.tensor.matmul(bilinear[m // 2][:, (m % 2) * BANK:(m % 2 + 1) * BANK],
                                                    w1_sb[:, q, m * P:(m + 1) * P], zt[:, q, c * BANK:(c + 1) * BANK],
                                                    start=(q == 0), stop=(q == KTILES - 1))
                        last.then_inc(h1_made, 1)
                for c in range(CHUNKS):
                    pe.wait_ge(h1_kept, half * (CHUNKS * 4) + 4 * (c + 1))
                    if c >= 1:
                        pe.wait_ge(h2_kept, half * (CHUNKS * 2) + 2 * c)
                    for m in range(HID2 // P):
                        for q in range(HID1 // P):
                            last = nc.tensor.matmul(turned[:, m * BANK:(m + 1) * BANK],
                                                    w2_sb[:, q, m * P:(m + 1) * P], h1[:, q, c * BANK:(c + 1) * BANK],
                                                    start=(q == 0), stop=(q == HID1 // P - 1))
                        last.then_inc(h2_made, 1)
                for c in range(CHUNKS):
                    pe.wait_ge(h2_kept, half * (CHUNKS * 2) + 2 * (c + 1))
                    for q in range(HID2 // P):
                        last = nc.tensor.matmul(sums[32:33, c * BANK:(c + 1) * BANK], w3_sb[:, q:q + 1],
                                                h2[:, q, c * BANK:(c + 1) * BANK],
                                                start=(q == 0), stop=(q == HID2 // P - 1))
                    last.then_inc(y_made, 1)
                pe.wait_ge(y_kept, half * CHUNKS + CHUNKS)


def kernel(**inputs):
    import concourse.bacc as bacc
    from concourse.bass_utils import run_bass_kernel_spmd

    rows, _ = rows_of_top1()
    nc = bacc.Bacc("TRN2", target_bir_lowering=False, num_devices=1)
    arrays, aps = {}, {}
    names = ["dense_ctx", "ids", *(f"tbl_{f}" for f in range(FIELDS)), "L0_rec_kernel",
             "W_top1", "b_top1", "W_top2", "b_top2", "W_top3"]
    for name in names:
        a = np.ascontiguousarray(inputs[name])
        if name == "W_top1":
            a = np.ascontiguousarray(a[rows])
        arrays[f"in_{name}"] = a
        aps[name] = nc.dram_tensor(f"in_{name}", a.shape, mybir.dt.from_np(a.dtype), kind="ExternalInput").ap()
    out = nc.dram_tensor("out_y", [BATCH, 1], F32, kind="ExternalOutput").ap()
    tower_kernel(nc, aps["dense_ctx"], aps["ids"], [aps[f"tbl_{f}"] for f in range(FIELDS)],
                 aps["L0_rec_kernel"], aps["W_top1"], aps["b_top1"], aps["W_top2"], aps["b_top2"],
                 aps["W_top3"], out)
    return run_bass_kernel_spmd(nc, [arrays], core_ids=[0]).results[0]["out_y"]
```

```python
from contextlib import ExitStack

import numpy as np

import concourse.bass as bass
from concourse import mybir

BATCH = 2048
FIELDS = 32
EMBED = 64
DENSE = 16
HID1 = 512
HID2 = 256

P = 128
PARTS = [512, 1024, 512]
WIDE = max(PARTS)
BANK = 512
SLOT = 2 * BANK
SLOTS = 3
STEPS = FIELDS - 1
PAIRS = FIELDS // 2
STAGES = 3
PAIR_SLOTS = PAIRS + 1
FEEDS = 2
AHEAD = 1
PRODUCT_COLS = 8 * WIDE
PREPS_FIRST = 4
PREP_AHEAD = 4
K_LO_AT, TURN_AT, SPLIT_AT = 0, 0, 2
MLP_FROM, MLP_PER_STEP = 2, 1
GROUP = 4
K_COLS = FIELDS * EMBED
PREP = 1024

F32 = mybir.dt.float32
F32R = mybir.dt.float32r
I32 = mybir.dt.int32
ALU = mybir.AluOpType
ACTF = mybir.ActivationFunctionType

PART_AT = [sum(PARTS[:n]) for n in range(len(PARTS))]
CHUNKS = [-(-w // BANK) for w in PARTS]
CHUNK = [w // c for w, c in zip(PARTS, CHUNKS)]
BLOCKS = [w // P for w in PARTS]
PER_BANK = [BANK // w for w in CHUNK]
BUNDLE = [2 * b // c for b, c in zip(PER_BANK, CHUNKS)]
RING = [PRODUCT_COLS // w // GROUP * GROUP for w in PARTS]
assert sum(PARTS) == BATCH and max(CHUNKS) <= 2


def tiles_of(j):
    return (j + 1) // 2


def tiles_until(j):
    return sum(tiles_of(s) for s in range(1, j + 1))


TILES = tiles_until(STEPS)
SUM_ROWS = TILES * 2
KTILES = SUM_ROWS // P
KTILE = TILES // KTILES
GROUPS = TILES // GROUP
PREPS = TILES * P // (2 * PREP)
assert SUM_ROWS == HID1 and SUM_ROWS % P == 0


def tile_number(n, j, p):
    return n * TILES + tiles_until(j - 1) + p


def pair_number(n, p):
    return n * PAIRS + p


def sums_until(n, g, c):
    return GROUPS * sum(CHUNKS[:n]) + g * CHUNKS[n] + c + 1


def pair_index(i, j):
    return i * (FIELDS - 1) - i * (i - 1) // 2 + (j - i - 1)


def sum_row(t):
    return t // KTILE, 32 * (t % GROUP) + 2 * (t % KTILE // GROUP)


def rows_of_top1():
    rows, spare = np.zeros(SUM_ROWS, np.int64), []
    for j in range(1, FIELDS):
        for p in range(tiles_of(j)):
            q, at = sum_row(tile_number(0, j, p))
            for s in range(2):
                if 2 * p + s < j:
                    rows[P * q + at + s] = pair_index(2 * p + s, j)
                else:
                    rows[P * q + at + s] = FIELDS * (FIELDS - 1) // 2 + len(spare)
                    spare.append(P * q + at + s)
    assert len(spare) == DENSE
    return rows, spare


def k_at(j):
    return P * tiles_until(j - 1)


def k_cols(j):
    return P * tiles_of(j)


def bundles_of(n, j):
    bundles, p = [], 0
    while p < tiles_of(j):
        size = 1
        while (size < BUNDLE[n] and p + size < tiles_of(j)
               and (tiles_until(j - 1) + p + size) % RING[n]
               and pair_number(n, p + size) % PAIR_SLOTS):
            size += 1
        bundles.append((p, size))
        p += size
    return bundles


def make_plan():
    steps = [(n, j) for n in range(len(PARTS)) for j in range(1, FIELDS)]

    def pair_for(s):
        if s < len(steps):
            n, j = steps[s]
            if j == 1 or j % 2 == 0:
                return n, j // 2

    plan = [(what, m) for m in range(PREPS_FIRST) for what in ("k_hi", "k_lo")]
    preps = list(range(PREPS_FIRST, PREPS))
    for s in range(AHEAD + 1):
        if pair_for(s):
            plan += [("turn", *pair_for(s)), ("split", *pair_for(s))]
        if s < AHEAD:
            plan.append(("feed", *steps[s]))
    plan += [("load", *steps[s]) for s in range(FEEDS - 1)]
    waiting = []
    left = []
    for n in range(len(PARTS)):
        sums = [(n, g, c) for g in range(GROUPS) for c in range(CHUNKS[n])]

        def sum_next(sums):
            n, g, c = sums.pop(0)
            plan.append(("sum", n, g, c))
            if (g + 1) * GROUP % KTILE == 0:
                q = (g + 1) * GROUP // KTILE - 1
                plan.append(("z", n, q, c))
                if c == CHUNKS[n] - 1:
                    plan.append(("dense", n, q))

        starts = []
        for j in range(1, FIELDS):
            s = n * STEPS + j - 1
            begun = []
            while preps and k_at(min(j + PREP_AHEAD + 1, FIELDS)) > preps[0] * 2 * PREP:
                begun.append(preps.pop(0))
                plan.append(("k_hi", begun[-1]))
            if s + AHEAD < len(steps):
                plan.append(("feed", *steps[s + AHEAD]))
            if s + FEEDS - 1 < len(steps):
                plan.append(("load", *steps[s + FEEDS - 1]))
            if j >= MLP_FROM:
                for _ in range(MLP_PER_STEP):
                    if waiting:
                        plan.append(waiting.pop(0))
            bundles = bundles_of(n, j)
            last = len(bundles) - 1
            turned = pair_for(s + AHEAD + 1)
            for k, (p, size) in enumerate(bundles):
                starts.append(tiles_until(j - 1) + p)
                plan.append(("tile", n, j, p, size))
                while left:
                    sum_next(left)
                while sums and len(starts) >= 4 and GROUP * (sums[0][1] + 1) <= starts[-2 - 2 * sums[0][2]]:
                    sum_next(sums)
                if k == min(K_LO_AT, last):
                    plan += [("k_lo", m) for m in begun]
                if turned and k == min(TURN_AT, last):
                    plan.append(("turn", *turned))
                if turned and k == min(SPLIT_AT, last):
                    plan.append(("split", *turned))
        left = sums
        for c in range(CHUNKS[n]):
            waiting += [("mlp", n, c, 1, m) for m in range(HID1 // P)]
            waiting += [("mlp", n, c, 2, m) for m in range(HID2 // P)]
            waiting += [("mlp", n, c, 3, 0), ("y", n, c)]
    while left:
        sum_next(left)
    return plan + waiting


PLAN = make_plan()
UNITS = [x[1:] for x in PLAN if x[0] == "mlp"]
SLOTTED = [x for x in PLAN if x[0] in ("tile", "turn", "mlp")]
SLOT_OF = {x: k for k, x in enumerate(SLOTTED)}
RESULTS = [x[1:] for x in PLAN if x[0] == "y"]
KEPT = [x[1:] for x in PLAN if x[0] == "z"]


def sum_bank(n, q, c):
    return c if CHUNKS[n] == 2 else q % 2


def tower_kernel(nc, dense_t, ids, tables, k_rec, w1, b1, w2, b2, w3, out):
    spare_in = [[(d, row) for d, row in enumerate(rows_of_top1()[1]) if row // P == q] for q in range(KTILES)]
    ctx = ExitStack()
    with ctx:
        def sb(name, shape, dt=F32):
            return ctx.enter_context(nc.sbuf_tensor(name, shape, dt))

        def sem(name):
            return ctx.enter_context(nc.semaphore(name))

        k_store = nc.dram_tensor("k_store", [P, TILES * P], F32, kind="Internal").ap()

        pair_emb = sb("pair_emb", [P, PAIR_SLOTS, WIDE])
        pair_hi = sb("pair_hi", [P, 2, WIDE], F32R)
        pair_lo = sb("pair_lo", [P, 2, WIDE], F32R)
        emb_hi = sb("emb_hi", [P, FEEDS, WIDE], F32R)
        emb_lo = sb("emb_lo", [P, FEEDS, WIDE], F32R)
        k_split = sb("k_split", [P, FEEDS, K_COLS], F32R)
        product = sb("product", [P, PRODUCT_COLS])
        stage = sb("stage", [P, STAGES, max(BLOCKS), 2, EMBED])
        zt = sb("zt", [P, KTILES, WIDE])
        h1 = sb("h1", [P, HID1 // P, max(CHUNK)])
        h2 = sb("h2", [P, HID2 // P, max(CHUNK)])
        w1_sb = sb("w1_sb", [P, KTILES, HID1])
        w2_sb = sb("w2_sb", [P, HID1 // P, HID2])
        w3_sb = sb("w3_sb", [P, HID2 // P])
        b1_sb = sb("b1_sb", [P, HID1 // P])
        b2_sb = sb("b2_sb", [P, HID2 // P])
        ids_sb = sb("ids_sb", [P, BATCH // P, FIELDS], I32)
        ident = sb("ident", [P, P])
        ones_sel = sb("ones_sel", [P, 62])
        y_sb = sb("y_sb", [1, 2, max(CHUNK)])
        free = WIDE - PARTS[0]
        prep_slots = -(-PREP // free)
        prep_cols = PREP // prep_slots
        assert 4 * prep_slots <= PAIRS and prep_cols * prep_slots == PREP and 2 * PREP <= KTILES * HID1

        def prep_raw(m):
            at = m % 2 * PREP
            return w1_sb[:, :, :].rearrange("p q n -> p (q n)")[:, at:at + PREP].rearrange("p (x n) -> p x n", n=prep_cols)

        def prep_part(part, m):
            at = (2 * part + m % 2) * prep_slots
            return pair_emb[:, at:at + prep_slots, PARTS[0]:PARTS[0] + prep_cols]

        products_ps = ctx.enter_context(nc.psum_tensor("products_ps", [P, SLOTS * SLOT], F32))
        sums_ps = ctx.enter_context(nc.psum_tensor("sums_ps", [P, 2, BANK], F32))

        def slot_ps(x):
            k, n = SLOT_OF[x] % SLOTS, x[1]
            pitch = CHUNK[n] if PER_BANK[n] > 1 else BANK
            return products_ps[:, k * SLOT:(k + 1) * SLOT].rearrange("p (x n) -> p x n", n=pitch)[:, :, 0:CHUNK[n]]

        def turned_at(n, p):
            at = SLOT_OF["turn", n, p] % SLOTS * SLOT
            return products_ps[:, at:at + PARTS[n]]

        ids_in = sem("ids_in")
        weights_in = sem("weights_in")
        consts = sem("consts")
        ident_cleared = sem("ident_cleared")
        sel_cleared = sem("sel_cleared")
        gathered = [sem(f"gathered{s}") for s in range(STAGES)]
        pair_turned = sem("pair_turned")
        pair_ready = sem("pair_ready")
        hi_ready = sem("hi_ready")
        lo_ready = sem("lo_ready")
        emb_fed = [sem(f"emb_fed{s}") for s in range(FEEDS)]
        own_fed = sem("own_fed")
        k_raw_in = [sem(f"k_raw_in{s}") for s in range(2)]
        k_hi_ready = sem("k_hi_ready")
        k_lo_ready = sem("k_lo_ready")
        k_stored = [sem(f"k_stored{s}") for s in range(2)]
        k_loaded = [sem(f"k_loaded{s}") for s in range(FEEDS)]
        tile_made = sem("tile_made")
        multiplied = sem("multiplied")
        summed = sem("summed")
        z_copied = sem("z_copied")
        dense_placed = [sem(f"dense_placed{q}") for q in range(KTILES)]
        unit_made = sem("unit_made")
        unit_kept = sem("unit_kept")
        y_out = [sem(f"y_out{s}") for s in range(2)]

        def gathers_until(n, p):
            r = pair_number(n, p)
            return sum(2 * BLOCKS[x // PAIRS] for x in range(r % STAGES, r + 1, STAGES))

        def step_number(n, j):
            return n * STEPS + j - 1

        def tiles_before_step(s):
            n, j = s // STEPS, s % STEPS + 1
            return n * TILES + tiles_until(j)

        def wait_pair_fed(engine, r):
            n, p = r // PAIRS, r % PAIRS
            for j in (2 * p, 2 * p + 1):
                if j >= 1:
                    s = step_number(n, j)
                    engine.wait_ge(emb_fed[s % FEEDS], 16 * 2 * (s // FEEDS + 1))

        def wait_stored(engine, m):
            for k in (m - 1, m):
                if k >= 0:
                    engine.wait_ge(k_stored[k % 2], 16 * 4 * (k // 2 + 1))

        block = ctx.enter_context(nc.Block())

        @block.sync
        def _(sp):
            def load_k_raw(m):
                if m >= 2:
                    sp.wait_ge(k_lo_ready, m - 1)
                sp.dma_start(prep_raw(m), k_rec[m].rearrange("p (x n) -> p x n", n=prep_cols)).then_inc(k_raw_in[m % 2], 16)

            sp.dma_start(ids_sb[:, :, :], ids).then_inc(ids_in, 16)
            load_k_raw(0)
            load_k_raw(1)
            sp.dma_start(w2_sb[:, :, :], w2.rearrange("(q p) n -> p q n", p=P)).then_inc(weights_in, 16)
            with nc.allow_non_contiguous_dma(reason="a few hundred values"):
                sp.dma_start(w3_sb[:, :], w3.rearrange("(q p) o -> p (q o)", p=P)).then_inc(weights_in, 16)
                sp.dma_start(b1_sb[:, :], b1.rearrange("(q p) -> p q", p=P)).then_inc(weights_in, 16)
                sp.dma_start(b2_sb[:, :], b2.rearrange("(q p) -> p q", p=P)).then_inc(weights_in, 16)
            for what, *x in PLAN:
                if what == "load":
                    n, j = x
                    s = step_number(n, j)
                    if s >= FEEDS:
                        sp.wait_ge(tile_made, tiles_before_step(s - FEEDS))
                    if n == 0:
                        wait_stored(sp, (k_at(j) + k_cols(j) - 1) // (2 * PREP))
                    sp.dma_start(k_split[:, s % FEEDS, 0:k_cols(j)].bitcast(F32),
                                 k_store[:, k_at(j):k_at(j) + k_cols(j)]).then_inc(k_loaded[s % FEEDS], 16)
                elif what == "feed":
                    n, j = x
                    s, w = step_number(n, j), PARTS[n]
                    if s >= FEEDS:
                        sp.wait_ge(tile_made, tiles_before_step(s - FEEDS))
                    r = pair_number(n, j // 2)
                    sp.wait_ge(lo_ready, r + 1)
                    own = slice(EMBED * (j % 2), EMBED * (j % 2) + EMBED)
                    other = slice(EMBED - own.start, EMBED - own.start + EMBED)
                    for part, to in ((pair_hi, emb_hi), (pair_lo, emb_lo)):
                        sp.dma_start(to[other, s % FEEDS, 0:w].bitcast(F32),
                                     part[own, r % 2, 0:w].bitcast(F32)).then_inc(emb_fed[s % FEEDS], 16)
                elif what == "y":
                    n, c = x
                    k, at, w = RESULTS.index((n, c)), PART_AT[n] + c * CHUNK[n], CHUNK[n]
                    sp.wait_ge(unit_kept, UNITS.index((n, c, 3, 0)) + 1)
                    sp.dma_start(out[:, at:at + w], y_sb[:, k % 2, 0:w]).then_inc(y_out[k % 2], 16)
                elif what == "k_lo":
                    m, = x
                    sp.wait_ge(k_lo_ready, m + 1)
                    for part in range(2):
                        for half in range(2):
                            cols = slice((2 * m + half) * PREP, (2 * m + half + 1) * PREP)
                            sp.dma_start(k_store[EMBED * part:EMBED * (part + 1), cols].rearrange("p (x n) -> p x n", n=prep_cols),
                                         prep_part(part, m)[EMBED * half:EMBED * (half + 1)]).then_inc(k_stored[m % 2], 16)
                    if m + 2 < PREPS:
                        load_k_raw(m + 2)
                    if m == PREPS - 1:
                        sp.dma_start(w1_sb[:, :, :], w1.rearrange("(q p) n -> p q n", p=P)).then_inc(weights_in, 16)
                elif what == "dense":
                    n, q = x
                    sp.wait_ge(z_copied, KEPT.index((n, q, CHUNKS[n] - 1)) + 1)
                    for d, row in spare_in[q]:
                        sp.dma_start(zt[row % P:row % P + 1, row // P, 0:PARTS[n]],
                                     dense_t[d:d + 1, PART_AT[n]:PART_AT[n] + PARTS[n]]).then_inc(dense_placed[q], 16)
            for k in range(2):
                sp.wait_ge(y_out[k], 16 * len(RESULTS[k::2]))

        @block.gpsimd
        def _(pool):
            nc.gpsimd.memset(ident[:, :], 0.0).then_inc(ident_cleared, 1)
            pool.wait_ge(ident_cleared, 1)
            nc.gpsimd.affine_select(out=ident[:, :], in_=ident[:, :], compare_op=ALU.not_equal, fill=1.0,
                                    base=0, pattern=[[-1, P]], channel_multiplier=1).then_inc(consts, 1)
            pool.wait_ge(ids_in, 16)
            for n in range(len(PARTS)):
                for p in range(PAIRS):
                    r = pair_number(n, p)
                    if r >= STAGES:
                        pool.wait_ge(pair_turned, r - STAGES + 1)
                    for f in range(2):
                        for t in range(BLOCKS[n]):
                            nc.gpsimd.indirect_dma_start(
                                stage[:, r % STAGES, t, f, :], None, tables[2 * p + f],
                                bass.IndirectOffsetOnAxis(
                                    ap=ids_sb[:, PART_AT[n] // P + t, 2 * p + f:2 * p + f + 1], axis=0),
                            ).then_inc(gathered[r % STAGES], 16)

        @block.scalar
        def _(act):
            for what, *x in PLAN:
                if what == "k_hi":
                    m, = x
                    act.wait_ge(k_raw_in[m % 2], 16 * (m // 2 + 1))
                    if m >= 2:
                        act.wait_ge(k_stored[m % 2], 16 * 4 * (m // 2))
                    nc.scalar.activation(prep_part(0, m).bitcast(F32R), prep_raw(m), ACTF.Copy).then_inc(k_hi_ready, 1)
                elif what == "turn":
                    n, p = x
                    r, w = pair_number(n, p), PARTS[n]
                    act.wait_ge(pair_turned, r + 1)
                    if n == 1:
                        wait_stored(act, PREPS - 1)
                    if r >= PAIR_SLOTS:
                        before = r - PAIR_SLOTS
                        act.wait_ge(multiplied, tile_number(before // PAIRS, STEPS, before % PAIRS) + 1)
                    nc.scalar.activation(pair_emb[:, r % PAIR_SLOTS, 0:w], turned_at(n, p), ACTF.Copy).then_inc(pair_ready, 1)
                    if r >= 2:
                        wait_pair_fed(act, r - 2)
                    nc.scalar.activation(pair_hi[:, r % 2, 0:w], turned_at(n, p), ACTF.Copy).then_inc(hi_ready, 1)
                elif what == "feed":
                    n, j = x
                    s, w, r = step_number(n, j), PARTS[n], pair_number(n, j // 2)
                    act.wait_ge(lo_ready, r + 1)
                    if s >= FEEDS:
                        act.wait_ge(tile_made, tiles_before_step(s - FEEDS))
                    own = slice(EMBED * (j % 2), EMBED * (j % 2) + EMBED)
                    nc.scalar.activation(emb_hi[own, s % FEEDS, 0:w], pair_hi[own, r % 2, 0:w].bitcast(F32), ACTF.Copy)
                    nc.scalar.activation(emb_lo[own, s % FEEDS, 0:w], pair_lo[own, r % 2, 0:w].bitcast(F32), ACTF.Copy).then_inc(own_fed, 1)
                elif what == "z":
                    n, q, c = x
                    act.wait_ge(summed, sums_until(n, GROUPS // KTILES * (q + 1) - 1, c))
                    if n >= 1 and q == 0:
                        act.wait_ge(unit_made, UNITS.index((n - 1, CHUNKS[n - 1] - 1, 1, HID1 // P - 1)) + 1)
                    w = CHUNK[n]
                    nc.scalar.activation(zt[:, q, c * w:(c + 1) * w], sums_ps[:, sum_bank(n, q, c), 0:w], ACTF.Copy).then_inc(z_copied, 1)
                elif what == "mlp":
                    n, c, layer, m = x
                    act.wait_ge(unit_made, UNITS.index((n, c, layer, m)) + 1)
                    if n == 0 and c == 0 and layer == 1 and m == 0:
                        act.wait_ge(weights_in, 16 * 5)
                    ps, w = slot_ps((what, *x))[:, 0, :], CHUNK[n]
                    if layer == 1:
                        nc.scalar.activation(h1[:, m, 0:w], ps, ACTF.Relu, bias=b1_sb[:, m:m + 1]).then_inc(unit_kept, 1)
                    elif layer == 2:
                        nc.scalar.activation(h2[:, m, 0:w], ps, ACTF.Relu, bias=b2_sb[:, m:m + 1]).then_inc(unit_kept, 1)
                    else:
                        k = RESULTS.index((n, c))
                        if k >= 2:
                            act.wait_ge(y_out[k % 2], 16 * (k // 2))
                        nc.scalar.activation(y_sb[:, k % 2, 0:w], ps[0:1, :], ACTF.Copy).then_inc(unit_kept, 1)

        @block.vector
        def _(dve):
            nc.vector.memset(ones_sel[:, :], 0.0).then_inc(sel_cleared, 1)
            dve.wait_ge(sel_cleared, 1)
            nc.vector.memset(ones_sel[0:EMBED, 30:31], 1.0).then_inc(consts, 1)
            nc.vector.memset(ones_sel[EMBED:P, 31:32], 1.0).then_inc(consts, 1)
            for what, *x in PLAN:
                if what == "k_lo":
                    m, = x
                    dve.wait_ge(k_hi_ready, m + 1)
                    nc.vector.tensor_tensor(prep_part(1, m).bitcast(F32R), prep_raw(m), prep_part(0, m),
                                            ALU.subtract).then_inc(k_lo_ready, 1)
                elif what == "split":
                    n, p = x
                    r, w = pair_number(n, p), PARTS[n]
                    dve.wait_ge(hi_ready, r + 1)
                    nc.vector.tensor_tensor(pair_lo[:, r % 2, 0:w], pair_emb[:, r % PAIR_SLOTS, 0:w], pair_hi[:, r % 2, 0:w].bitcast(F32),
                                            ALU.subtract).then_inc(lo_ready, 1)
                elif what == "tile":
                    n, j, p, size = x
                    t, w = tiles_until(j - 1) + p, PARTS[n]
                    if p == 0:
                        dve.wait_ge(pair_ready, pair_number(n, tiles_of(j) - 1) + 1)
                    dve.wait_ge(tile_made, n * TILES + t + size)
                    if t + size > RING[n]:
                        dve.wait_ge(summed, sums_until(n, (t + size - 1 - RING[n]) // GROUP, CHUNKS[n] - 1))
                    elif n >= 1:
                        dve.wait_ge(summed, sums_until(n - 1, GROUPS - 1, CHUNKS[n - 1] - 1))
                    at = pair_number(n, p) % PAIR_SLOTS
                    if CHUNKS[n] == 1:
                        pairs = pair_emb[:, at:at + size, 0:w]
                    else:
                        pairs = pair_emb[:, at, 0:w].rearrange("p (x n) -> p x n", n=CHUNK[n])
                    kept = product[:, t % RING[n] * w:(t % RING[n] + size) * w].rearrange("p (x n) -> p x n", n=CHUNK[n])
                    nc.vector.tensor_tensor(kept, slot_ps((what, *x))[:, 0:size * CHUNKS[n], :], pairs,
                                            ALU.mult).then_inc(multiplied, size)

        @block.tensor
        def _(pe):
            pe.wait_ge(consts, 3)

            def claim_slot(x):
                k = SLOT_OF[x]
                if k >= SLOTS:
                    before = SLOTTED[k - SLOTS]
                    if before[0] == "tile":
                        _, n, j, p, size = before
                        pe.wait_ge(multiplied, tile_number(n, j, p) + size)
                    elif before[0] == "turn":
                        pe.wait_ge(hi_ready, pair_number(*before[1:]) + 1)
                    else:
                        pe.wait_ge(unit_kept, UNITS.index(before[1:]) + 1)

            for what, *x in PLAN:
                if what == "turn":
                    n, p = x
                    r = pair_number(n, p)
                    pe.wait_ge(gathered[r % STAGES], 16 * gathers_until(n, p))
                    claim_slot((what, *x))
                    for t in range(BLOCKS[n]):
                        rows = stage[:, r % STAGES, t, :, :].rearrange("p f e -> p (f e)")
                        last = nc.tensor.transpose(turned_at(n, p)[:, t * P:(t + 1) * P], rows, ident[:, :])
                    last.then_inc(pair_turned, 1)
                elif what == "tile":
                    n, j, p, size = x
                    s, w = step_number(n, j), CHUNK[n]
                    if p == 0:
                        pe.wait_ge(emb_fed[s % FEEDS], 16 * 2 * (s // FEEDS + 1))
                        pe.wait_ge(own_fed, s + 1)
                        pe.wait_ge(k_loaded[s % FEEDS], 16 * (s // FEEDS + 1))
                    claim_slot((what, *x))
                    ps = slot_ps((what, *x))
                    for k in range(size):
                        weights = k_split[:, s % FEEDS, (p + k) * P:(p + k + 1) * P]
                        for c in range(CHUNKS[n]):
                            cols = slice(c * w, (c + 1) * w)
                            to = ps[:, k * CHUNKS[n] + c, :]
                            nc.tensor.matmul(to, weights, emb_lo[:, s % FEEDS, cols], start=True, stop=False)
                            last = nc.tensor.matmul(to, weights, emb_hi[:, s % FEEDS, cols], start=False, stop=True)
                    last.then_inc(tile_made, size)
                elif what == "sum":
                    n, g, c = x
                    pe.wait_ge(multiplied, n * TILES + GROUP * (g + 1))
                    q, row = sum_row(GROUP * g)
                    bank, w = sum_bank(n, q, c), CHUNK[n]
                    if row == 0:
                        before = [k for k, y in enumerate(KEPT[:KEPT.index((n, q, c))]) if sum_bank(*y) == bank]
                        if before:
                            pe.wait_ge(z_copied, before[-1] + 1)
                    for k in range(GROUP):
                        at = (GROUP * g + k) % RING[n] * PARTS[n] + c * w
                        last = nc.tensor.matmul(sums_ps[32 * k:32 * k + 32, bank, 0:w], ones_sel[:, 30 - row:62 - row],
                                                product[:, at:at + w], start=(row == 0), stop=(row == 30))
                    last.then_inc(summed, 1)
                elif what == "mlp":
                    n, c, layer, m = x
                    u = UNITS.index((n, c, layer, m))
                    if layer == 1 and m == 0:
                        pe.wait_ge(weights_in, 16 * 5)
                    elif m == 0:
                        pe.wait_ge(unit_kept, u)
                    claim_slot((what, *x))
                    ps, w = slot_ps((what, *x))[:, 0, :], CHUNK[n]
                    cols = slice(m * P, (m + 1) * P)
                    if layer == 1:
                        terms = [(w1_sb[:, q, cols], zt[:, q, c * w:(c + 1) * w]) for q in range(KTILES)]
                    elif layer == 2:
                        terms = [(w2_sb[:, q, cols], h1[:, q, 0:w]) for q in range(HID1 // P)]
                    else:
                        terms = [(w3_sb[:, q:q + 1], h2[:, q, 0:w]) for q in range(HID2 // P)]
                    to = ps[0:1, :] if layer == 3 else ps
                    for k, (weights, moving) in enumerate(terms):
                        if layer == 1 and m == 0:
                            pe.wait_ge(z_copied, KEPT.index((n, k, c)) + 1)
                            pe.wait_ge(dense_placed[k], 16 * len(spare_in[k]) * (n + 1))
                        last = nc.tensor.matmul(to, weights, moving, start=(k == 0), stop=(k == len(terms) - 1))
                    last.then_inc(unit_made, 1)


def kernel(**inputs):
    import concourse.bacc as bacc
    from concourse.bass_utils import run_bass_kernel_spmd

    rows, _ = rows_of_top1()
    k = np.asarray(inputs["L0_rec_kernel"])
    k_rec = np.zeros((EMBED, SUM_ROWS, EMBED), k.dtype)
    for j in range(1, FIELDS):
        at = k_at(j) // EMBED
        k_rec[:, at:at + j] = k[:, [pair_index(i, j) for i in range(j)]]
    k_rec = k_rec.reshape(EMBED, PREPS, 2, PREP).transpose(1, 2, 0, 3).reshape(PREPS, P, PREP)
    laid_out = {
        "dense_t": np.ascontiguousarray(np.asarray(inputs["dense_ctx"]).T),
        "ids": np.ascontiguousarray(np.asarray(inputs["ids"]).reshape(BATCH // P, P, FIELDS).transpose(1, 0, 2)),
        "k_rec": k_rec,
        "w1": np.ascontiguousarray(np.asarray(inputs["W_top1"])[rows]),
        "b1": inputs["b_top1"], "w2": inputs["W_top2"], "b2": inputs["b_top2"], "w3": inputs["W_top3"],
        **{f"tbl_{f}": inputs[f"tbl_{f}"] for f in range(FIELDS)},
    }
    nc = bacc.Bacc("TRN2", target_bir_lowering=False, num_devices=1)
    arrays, aps = {}, {}
    for name, a in laid_out.items():
        a = np.ascontiguousarray(a)
        arrays[f"in_{name}"] = a
        aps[name] = nc.dram_tensor(f"in_{name}", a.shape, mybir.dt.from_np(a.dtype), kind="ExternalInput").ap()
    out = nc.dram_tensor("out_y", [BATCH, 1], F32, kind="ExternalOutput").ap()
    tower_kernel(nc, aps["dense_t"], aps["ids"], [aps[f"tbl_{f}"] for f in range(FIELDS)], aps["k_rec"],
                 aps["w1"], aps["b1"], aps["w2"], aps["b2"], aps["w3"], out.rearrange("b o -> o b"))
    return run_bass_kernel_spmd(nc, [arrays], core_ids=[0]).results[0]["out_y"]
```
